# Optimizing a Trainium2 kernel written in Bass

```python
import numpy as np
import jax
import jax.numpy as jnp

def _softmax(x, axis=-1):
    return jax.nn.softmax(x, axis=axis)
def _gelu(x):
    return jax.nn.gelu(x, approximate=True)
def _silu(x):
    return jax.nn.silu(x)
def _sigmoid(x):
    return jax.nn.sigmoid(x)
def _layernorm(x, axis=-1, eps=1e-5):
    m = jnp.mean(x, axis=axis, keepdims=True)
    v = jnp.var(x, axis=axis, keepdims=True)
    return (x - m) / jnp.sqrt(v + eps)
def _scatter_add(tgt, idx, src, axis=0):
    return tgt.at[idx].add(src)
def _segment_sum(src, seg, n):
    return jax.ops.segment_sum(src, seg, n)

kernel_name = 'mk_conv_seq_d1_conv_nhwc256_c97385'

def setup_inputs(seed: int = 0):
    np.random.seed(seed)
    _w = jnp.asarray
    def _rec_inputs():
        import jax
        import jax.numpy as jnp
        _gk = jax.random.key(seed)
        x = -0.0005207 + 1.001 * jax.random.normal(jax.random.fold_in(_gk, 1), (8, 32, 32, 256), jnp.float32)
        return x
    x = _rec_inputs()
    def _L0_conv_setup():
        import jax, jax.numpy as jnp
        import numpy as np
        N_CHANNELS = 256
        N_HEADS = 4
        key = jax.random.key(seed)
        k_x, k_qkv, k_out, k_b = jax.random.split(key, 4)
        C, h = (N_CHANNELS, N_HEADS)
        x = jax.random.normal(k_x, (8, 32, 32, C), dtype=jnp.float32)
        W_qkv = jax.random.normal(k_qkv, (C, h * C * 3), dtype=jnp.float32) * C ** (-0.5)
        W_out = jax.random.normal(k_out, (h * C, C), dtype=jnp.float32) * (h * C) ** (-0.5)
        b_out = jnp.zeros((C,), dtype=jnp.float32)
        return {'x': x, 'W_qkv': W_qkv, 'W_out': W_out, 'b_out': b_out}
    _L0_conv_all = _L0_conv_setup()
    _L0_conv_in = {k: v for k, v in _L0_conv_all.items() if k in ('W_qkv', 'W_out', 'b_out', )}
    del _L0_conv_all

    return {
        "x": x,
        "L0_conv_W_qkv": _L0_conv_in["W_qkv"],
        "L0_conv_W_out": _L0_conv_in["W_out"],
        "L0_conv_b_out": _L0_conv_in["b_out"],
    }

def reference(x, L0_conv_W_qkv, L0_conv_W_out, L0_conv_b_out):
    import jax
    import jax.numpy as jnp
    def _L0_conv_ref(x, W_qkv, W_out, b_out):
        import jax, jax.numpy as jnp
        import numpy as np
        N_CHANNELS = 256
        N_HEADS = 4
        B, H, W, C = x.shape
        h = W_qkv.shape[1] // (3 * C)
        scale = C ** (-0.5)
        xf = x.reshape(B, -1, C)
        qkv = jnp.einsum('bnc,cd->bnd', xf, W_qkv)
        qkv = qkv.reshape(B, -1, h, 3 * C)
        q, k, v = jnp.split(qkv, 3, axis=-1)
        atten = jnp.einsum('bihd,bjhd->bijh', q, k) * scale
        atten = jax.nn.softmax(atten, axis=2)
        res = jnp.einsum('bijh,bjhd->bihd', atten, v)
        res = res.reshape(B, -1, h * C)
        res = jnp.einsum('bnd,dc->bnc', res, W_out) + b_out
        res = res + xf
        return res.reshape(B, H, W, C)

    def _gn(v, G=32, eps=1e-5):
        B_, H_, W_, C_ = v.shape
        g = v.reshape(B_, H_, W_, G, C_ // G)
        m = jnp.mean(g, axis=(1, 2, 4), keepdims=True)
        s = jnp.var(g, axis=(1, 2, 4), keepdims=True)
        return ((g - m) / jnp.sqrt(s + eps)).reshape(v.shape)

    def _ln_c(v, eps=1e-6):
        m = jnp.mean(v, axis=-1, keepdims=True)
        s = jnp.var(v, axis=-1, keepdims=True)
        return (v - m) / jnp.sqrt(s + eps)

    def _ln_t(v, eps=1e-5):
        m = jnp.mean(v, axis=-1, keepdims=True)
        s = jnp.var(v, axis=-1, keepdims=True)
        return (v - m) / jnp.sqrt(s + eps)

    def _to_tokens(v):
        B_, H_, W_, C_ = v.shape
        return v.reshape(B_, H_ * W_, C_)
    def _from_tokens(t, like):
        return t.reshape(like.shape)

    x = _L0_conv_ref(x, L0_conv_W_qkv, L0_conv_W_out, L0_conv_b_out)
    return x


_drawn_inputs = setup_inputs


def setup_inputs(seed=0):
    import zlib

    import numpy as np

    out = dict(_drawn_inputs(seed))
    spreads = {'L0_conv_b_out': (0.0, 0.1)}
    factors = {}
    for name, (base, spread) in spreads.items():
        noise = np.random.default_rng([zlib.crc32(name.encode()), seed]).standard_normal(out[name].shape)
        drawn = base * np.exp(spread * noise) if base else spread * noise
        out[name] = jnp.asarray(drawn.astype(out[name].dtype))
    for name, factor in factors.items():
        out[name] = (out[name] * factor).astype(out[name].dtype)
    return out
```

```python
from contextlib import ExitStack

import concourse.bass as bass
from concourse import mybir

ALU = mybir.AluOpType
ACT = mybir.ActivationFunctionType
AX = mybir.AxisListType
F32 = mybir.dt.float32
F16 = mybir.dt.float16
U32 = mybir.dt.uint32

P = 128
BANK = 512

S_BANK = 0
Y_BANK = 4
MISC_BANK = 6
XT_BANK = 7

TOP = 2.0 ** 14
TINY = 2.0 ** -80
EXP_MASK = 0x7F800000
LN2 = 0.6931471805599453
PROB_SHIFT = 14 * LN2


def attention(nc, x, w_qkv, w_out, b_out, out):
    B, H, W, C = x.shape
    N = H * W
    HEADS = w_out.shape[0] // C
    CT = C // P
    JT = N // P
    PAIRS = B * HEADS
    GROUP = N // 2
    GT = GROUP // P
    QUARTER = N // HEADS
    QT_TILES = QUARTER // P
    assert C == 2 * P and HEADS == 4 and N == 2 * BANK and GT == 4 and QT_TILES == 2

    Q_DOWN = 1.0 / (4 * C * TOP)
    Y_DOWN = 1.0 / (N * TOP)
    SCORE = C ** -0.5 / (Q_DOWN * TOP ** 3)
    RESULT = 1.0 / (Y_DOWN * TOP ** 2)

    with ExitStack() as ctx:
        def sb(name, shape, dt):
            return ctx.enter_context(nc.sbuf_tensor(name, shape, dt))

        def sem(name):
            return ctx.enter_context(nc.semaphore(name))

        XSIZE = CT * N
        ASIZE = HEADS * CT * C
        TILE = 2 * N
        x_res = sb("x_res", [P, B * JT * C], F32)
        x_nat = sb("x_nat", [P, 4 * XSIZE], F16)
        x_turn = sb("x_turn", [P, 4, CT, N], F16)
        probs = sb("probs", [P, 2, N], F32)
        probs_t = sb("probs_t", [P, 2, 2, JT, GROUP], F16)
        q_t = sb("q_t", [P, 2, CT, N], F16)
        y_t = sb("y_t", [P, 2, CT, GROUP], F16)
        a_w = sb("a_w", [P, 2 * ASIZE], F16)
        m_w = sb("m_w", [P, 2 * ASIZE], F16)
        wqkv = sb("wqkv", [P, CT, HEADS * 3 * C], F32)
        wo = sb("wo", [P, HEADS * CT, C], F32)
        probs_n = wqkv[:].rearrange("p s n -> p (s n)").bitcast(F16)[:, 0:2 * TILE].rearrange(
            "p (a i n) -> p a i n", a=2, i=2)
        bias = sb("bias", [P, C], F32)
        stage = sb("stage", [P, QT_TILES * C], F32)
        raw = sb("raw", [P, QT_TILES * C], F32)
        ident = sb("ident", [P, P], F32)
        ones = sb("ones", [P, P], F32)
        spread = sb("spread", [P, 3, P], F32)
        img_max = sb("img_max", [P, B], F32)
        cols = sb("cols", [P, 32], F32)
        row_max = sb("row_max", [P, 2], F32)
        exp_bias = sb("exp_bias", [P, 2], F32)
        row_sum = sb("row_sum", [P, 2, GT], F32)
        row_inv = sb("row_inv", [P, 2, GT], F32)
        row_fac = sb("row_fac", [P, 2, GT], F32)
        ps = ctx.enter_context(nc.psum_tensor("ps", [P, 8, BANK], F32))

        pt32 = probs_t[:].rearrange("p a b j i -> p (a b j i)").bitcast(F32)
        w_turn = pt32[:, 0:3 * HEADS * CT * C].rearrange("p (m h s c) -> p m h s c", m=3, h=HEADS, s=CT)
        stage0 = pt32[:, 3 * HEADS * CT * C:3 * HEADS * CT * C + JT * C]

        def col(i):
            return cols[:, i:i + 1]
        X0, A0, M0 = 0, 4, 8
        SC_A, SC_B, SCORE_COL, NEG_SCORE, RES_A, RES_COL = 12, 13, 14, 15, 16, 17
        X_SCALE, A_SCALE, M_SCALE = X0 + 3, A0 + 3, M0 + 3

        w_in = [sem(f"w_in{h}") for h in range(HEADS)]
        x_in = [sem(f"x_in{b}") for b in range(B)]
        wo_in, bias_in, stored = sem("wo_in"), sem("bias_in"), sem("stored")
        const_ready = sem("const_ready")
        w_kept_act, w_kept_dve = sem("w_kept_act"), sem("w_kept_dve")
        a_made, m_made = sem("a_made"), sem("m_made")
        a_high, a_split, m_high, m_split = sem("a_high"), sem("a_split"), sem("m_high"), sem("m_split")
        spread_ready, spread_turned = sem("spread_ready"), sem("spread_turned")
        scale_ready = sem("scale_ready")
        stage0_ready = sem("stage0_ready")
        dve_chain = sem("dve_chain")
        scores_made = sem("scores_made")
        y_made = sem("y_made")
        q_made = sem("q_made")
        out_made = sem("out_made")
        x_turned = sem("x_turned")
        probs_ready = sem("probs_ready")
        probs_high = sem("probs_high")
        y_high = sem("y_high")
        q_high = sem("q_high")
        xt_high = sem("xt_high")
        max_ready = sem("max_ready")
        exp_bias_ready = sem("exp_bias_ready")
        probs_split = sem("probs_split")
        y_split = sem("y_split")
        q_split = sem("q_split")
        xt_split = sem("xt_split")
        inv_ready = sem("inv_ready")
        fac_ready = sem("fac_ready")
        added = sem("added")
        probs_turned = [sem(f"probs_turned{i}") for i in range(2)]
        stage_ready = sem("stage_ready")
        raw_ready = sem("raw_ready")
        pool_chain = sem("pool_chain")
        xn_high = sem("xn_high")
        xn_split = sem("xn_split")
        turns_begun = sem("turns_begun")
        w_turned = sem("w_turned")

        x_dram = x.rearrange("b h w c -> (b h w) c").rearrange("(b t p) c -> b p t c", b=B, p=P)
        out_dram = out.rearrange("b h w c -> (b h w) c").rearrange("(g t p) c -> g p t c", g=2 * B, p=P)

        block = ctx.enter_context(nc.Block())

        @block.sync
        def _(sp):
            wsrc = w_qkv.rearrange("(s p) n -> p s n", p=P)
            for h in range(HEADS):
                cut = slice(h * 3 * C, (h + 1) * 3 * C)
                sp.dma_start(wqkv[:, :, cut], wsrc[:, :, cut]).then_inc(w_in[h], 16)
            sp.dma_start(wo[:], w_out.rearrange("(s p) c -> p s c", p=P)).then_inc(wo_in, 16)
            for b in range(B):
                dst = x_res[:, b * JT * C:(b + 1) * JT * C].rearrange("p (t c) -> p t c", c=C)
                sp.dma_start(dst, x_dram[b]).then_inc(x_in[b], 16)
            sp.dma_start(bias[:], b_out.rearrange("(a c) -> a c", a=1).broadcast_to([P, C])).then_inc(bias_in, 16)

            def turn_tile(k, half, t, later):
                f, parity = 2 * k + half, t % 2
                sp.wait_ge(probs_split, GT * f + t + 1)
                if t == 0 and later:
                    sp.wait_ge(y_made, 2 * (f - 2) + 2)
                sp.sem_inc(turns_begun, 1)
                dst = probs_t[:, half].rearrange("p i j q -> p (i j) q")[:, :, t * P:(t + 1) * P]
                src = probs_n[:, parity].rearrange("p i n -> p (i n)")
                sp.dma_start_transpose(dst, src).then_inc(probs_turned[parity], 16)

            def turn_pair(k, later):
                for half in range(2):
                    for t in range(GT):
                        turn_tile(k, half, t, later)

            def store(b, half):
                sp.wait_ge(added, 1 + GT * (2 * HEADS * b + 2 * HEADS - 1 + half))
                src = x_res[:, bass.ds((b * 2 + half) * GT * C, GT * C)].rearrange("p (t c) -> p t c", c=C)
                dst = out_dram[bass.ds(b * 2 + half, 1)].rearrange("g p t c -> p (g t) c")
                sp.dma_start(dst, src).then_inc(stored, 16)

            for h in range(HEADS):
                turn_pair(h, h > 0)
            with sp.Fori(1, B) as b:
                for h in range(HEADS):
                    turn_pair(HEADS * b + h, True)
                    if h == 1:
                        store(b - 1, 0)
                        store(b - 1, 1)
            store(B - 1, 0)
            store(B - 1, 1)
            sp.wait_ge(stored, 16 * 2 * B)

        @block.tensor
        def _(pe):
            def turn_weights(r, h, m):
                if r >= 4:
                    if r % 2 == 0:
                        pe.wait_ge(w_kept_act, (r - 4) // 2 + 1)
                    else:
                        pe.wait_ge(w_kept_dve, (r - 4) // 2 + 1)
                for s in range(CT):
                    for c in range(CT):
                        o = (h * 3 + m) * C + s * P
                        mm = pe.transpose(ps[:, 4 + r % 4, s * C + c * P:s * C + (c + 1) * P],
                                          wqkv[:, c, o:o + P], ident[:])
                mm.then_inc(w_turned, 1)

            def product(bank, left, right, done):
                for c in range(CT):
                    for s in range(CT):
                        mm = pe.matmul(ps[:, bank, c * C:(c + 1) * C], left[:, s, c * P:(c + 1) * P],
                                       right[:, s, :], start=(s == 0), stop=(s == CT - 1))
                mm.then_inc(done, 1)

            pe.wait_ge(const_ready, 3)
            for h in range(HEADS + 1):
                if h < HEADS:
                    pe.wait_ge(w_in[h], 16)
                    turn_weights(2 * h, h, 0)
                    turn_weights(2 * h + 1, h, 1)
                if h >= 1:
                    pe.wait_ge(w_kept_act, h)
                    pe.wait_ge(w_kept_dve, h)
                    product(h - 1, w_turn[:, 0, h - 1], w_turn[:, 1, h - 1], a_made)
            for h in range(HEADS):
                turn_weights(2 * HEADS + h, h, 2)
            pe.wait_ge(w_kept_act, 5)
            pe.wait_ge(spread_ready, 1)
            pe.transpose(ps[:, 4, 0:P], spread[:, 0, :], ident[:]).then_inc(spread_turned, 1)
            pe.wait_ge(w_kept_act, 6)
            pe.wait_ge(w_kept_dve, 6)
            pe.wait_ge(a_split, 1)
            pe.wait_ge(wo_in, 16)
            for h in range(HEADS):
                product(h, w_turn[:, 2, h], wo[:, h * CT:(h + 1) * CT, :], m_made)
            pe.wait_ge(spread_ready, 2)
            pe.transpose(ps[:, 5, 0:P], spread[:, 1, :], ident[:]).then_inc(spread_turned, 1)
            pe.wait_ge(spread_ready, 3)
            pe.transpose(ps[:, 6, 0:P], spread[:, 2, :], ident[:]).then_inc(spread_turned, 1)
            pe.wait_ge(m_split, 1)
            pe.wait_ge(stage0_ready, 1)
            for q in range(HEADS):
                for c in range(CT):
                    for j in range(QT_TILES):
                        o = (q * QT_TILES + j) * C + c * P
                        mm = pe.transpose(ps[:, q, c * QUARTER + j * P:c * QUARTER + (j + 1) * P],
                                          stage0[:, o:o + P], ident[:])
                mm.then_inc(x_turned, 1)

            a_flat, m_flat = a_w, m_w

            def parts():
                return ((0, 0), (0, 1), (1, 0))

            def q_bank(k_of, half, c2):
                head = (k_of % HEADS) * (CT * C)
                par = ((k_of // HEADS) % 2) * 2
                first = True
                for c in range(CT):
                    for l, r in parts():
                        lhs = a_flat[:, bass.ds(head + (l * ASIZE + c * C + c2 * P), P)]
                        rhs = x_turn[:].rearrange("p a c n -> p (a c n)")[
                            :, bass.ds(par * (CT * N) + ((r * CT + c) * N + half * GROUP), GROUP)]
                        mm = pe.matmul(ps[:, MISC_BANK, :], lhs, rhs, start=first,
                                       stop=(c == CT - 1 and (l, r) == (1, 0)))
                        first = False
                mm.then_inc(q_made, 1)

            def out_bank(k_of, pair):
                head = (k_of % HEADS) * (CT * C)
                for i in range(2):
                    q0 = (2 * pair + i) * P
                    first = True
                    for c in range(CT):
                        for l, r in parts():
                            mm = pe.matmul(ps[:, MISC_BANK, i * C:(i + 1) * C], y_t[:, l, c, q0:q0 + P],
                                           m_flat[:, bass.ds(head + (r * ASIZE + c * C), C)],
                                           start=first, stop=(c == CT - 1 and (l, r) == (1, 0)))
                            first = False
                mm.then_inc(out_made, 1)

            def scores(k, half, t):
                par = ((k // HEADS) % 2) * 2
                q0 = half * GROUP + t * P
                for j in range(2):
                    first = True
                    for c in range(CT):
                        for l, r in parts():
                            rhs = x_turn[:].rearrange("p a c n -> p (a c n)")[
                                :, bass.ds(par * (CT * N) + ((r * CT + c) * N + j * BANK), BANK)]
                            mm = pe.matmul(ps[:, S_BANK + 2 * (t % 2) + j, :], q_t[:, l, c, q0:q0 + P], rhs,
                                           start=first, stop=(c == CT - 1 and (l, r) == (1, 0)))
                            first = False
                mm.then_inc(scores_made, 1)

            def weigh(k_of, par_group, t, c):
                img = ((k_of // HEADS) % 2) * (2 * XSIZE)
                for j in (2 * t, 2 * t + 1):
                    for l, r in parts():
                        lhs = x_nat[:, bass.ds(img + (l * XSIZE + j * C + c * P), P)]
                        mm = pe.matmul(ps[:, Y_BANK + c, :], lhs, probs_t[:, par_group, r, j, :],
                                       start=(j == 0 and (l, r) == (0, 0)),
                                       stop=(j == JT - 1 and (l, r) == (1, 0)))
                return mm

            for c2 in range(CT):
                pe.wait_ge(xt_split, 2)
                if c2:
                    pe.wait_ge(q_split, c2)
                q_bank(0, 0, c2)

            def phase(k, half, later, prep, last):
                f = 2 * k + half
                for t in range(GT):
                    n = GT * f + t
                    if t == 0:
                        pe.wait_ge(q_split, 2 * f + 2)
                        pe.wait_ge(xt_split, HEADS * (k // HEADS) + 4)
                    if later or half or t >= 2:
                        pe.wait_ge(probs_high, n - 1)
                    scores(k, half, t)
                    if t < 2 and not (last and half):
                        if t == 0 and later:
                            pe.wait_ge(added, 1 + GT * (f - 2))
                        if t == 1:
                            pe.wait_ge(q_split, 2 * f + 3)
                        if t == 0 and half:
                            pe.wait_ge(xt_split, HEADS * ((k + 1) // HEADS) + 2)
                        q_bank(k + half, 1 - half, t)
                    if t >= 2 and later:
                        if t == 2:
                            if last and half:
                                pe.wait_ge(added, 1 + GT * (f - 2))
                            else:
                                pe.wait_ge(q_split, 2 * f + 4)
                            pe.wait_ge(y_split, 2 * (f - 2) + 2)
                        if t == 3:
                            pe.wait_ge(added, 1 + GT * (f - 2) + 2)
                        out_bank(k - 1, t - 2)
                    if prep and not half and t == 2:
                        pe.wait_ge(stage_ready, k + 1)
                        pe.wait_ge(xt_split, k + HEADS)
                        for c in range(CT):
                            for j in range(QT_TILES):
                                mm = pe.transpose(ps[:, XT_BANK, c * QUARTER + j * P:c * QUARTER + (j + 1) * P],
                                                  stage[:, j * C + c * P:j * C + (c + 1) * P], ident[:])
                        mm.then_inc(x_turned, 1)
                    if t == 0 and later:
                        for c in range(CT):
                            weigh(k - 1, half, GT - 1, c).then_inc(y_made, 1)
                    if t >= 1 and (later or half):
                        k_of = k if half else k - 1
                        if t == 1:
                            pe.wait_ge(probs_turned[0], 32 * f)
                            pe.wait_ge(probs_turned[1], 32 * f)
                            pe.wait_ge(xn_split, HEADS * (k_of // HEADS) + 4)
                        for c in range(CT):
                            if t == 1 and later:
                                pe.wait_ge(y_split, 2 * (f - 2) + c + 1)
                            weigh(k_of, 1 - half, t - 1, c)

            def pair(k, later, prep, last):
                phase(k, 0, later, prep, last)
                phase(k, 1, later, prep, last)

            pair(0, False, True, False)
            with pe.Fori(1, PAIRS - HEADS) as k:
                pair(k, True, True, False)
            with pe.Fori(PAIRS - HEADS, PAIRS - 1) as k:
                pair(k, True, False, False)
            pair(PAIRS - 1, True, False, True)

            f = 2 * PAIRS
            for c in range(CT):
                weigh(PAIRS - 1, 0, GT - 1, c).then_inc(y_made, 1)
            pe.wait_ge(y_split, 2 * (f - 2) + 2)
            for i in range(2):
                pe.wait_ge(added, 1 + GT * (f - 2) + 2 * i)
                out_bank(PAIRS - 1, i)
            pe.wait_ge(probs_turned[0], 32 * f)
            pe.wait_ge(probs_turned[1], 32 * f)
            for c in range(CT):
                for t in range(GT):
                    mm = weigh(PAIRS - 1, 1, t, c)
                mm.then_inc(y_made, 1)
            pe.wait_ge(y_split, 2 * (f - 1) + 2)
            for i in range(2):
                pe.wait_ge(added, 1 + GT * (f - 1) + 2 * i)
                out_bank(PAIRS - 1, i)

        @block.scalar
        def _(act):
            def keep(r, i, h, m):
                act.wait_ge(w_turned, r + 1)
                act.activation(w_turn[:, m, h].rearrange("p s c -> p (s c)"), ps[:, 4 + r % 4, :],
                               ACT.Copy).then_inc(w_kept_act, 1)

            for h in range(HEADS):
                keep(2 * h, h, h, 0)
            keep(2 * HEADS, HEADS, 0, 2)
            keep(2 * HEADS + 2, HEADS + 1, 2, 2)
            act.wait_ge(scale_ready, 1)
            act.activation(a_w[:, 0:ASIZE], ps[:, 0:HEADS, :].rearrange("p h n -> p (h n)"), ACT.Copy,
                           scale=col(A_SCALE)).then_inc(a_high, 1)
            act.wait_ge(scale_ready, 2)
            act.activation(m_w[:, 0:ASIZE], ps[:, 0:HEADS, :].rearrange("p h n -> p (h n)"), ACT.Copy,
                           scale=col(M_SCALE)).then_inc(m_high, 1)

            def xt_quarter(bank, par, q, done):
                act.wait_ge(x_turned, done)
                act.activation(x_turn[:, bass.ds(par, 1), :, bass.ds(q * QUARTER, QUARTER)].rearrange(
                    "p a c n -> p (a c) n"), ps[:, bank, :].rearrange("p (c n) -> p c n", c=CT),
                    ACT.Copy).then_inc(xt_high, 1)

            def q_part(half, c2, done):
                act.wait_ge(q_made, done)
                act.activation(q_t[:, 0, c2, half * GROUP:(half + 1) * GROUP], ps[:, MISC_BANK, :],
                               ACT.Copy, scale=Q_DOWN).then_inc(q_high, 1)

            def y_parts(g):
                for c in range(CT):
                    act.wait_ge(y_made, 2 * g + c + 1)
                    act.activation(y_t[:, 0, c, :], ps[:, Y_BANK + c, :], ACT.Copy,
                                   scale=Y_DOWN).then_inc(y_high, 1)

            for q in range(HEADS):
                xt_quarter(q, 0, q, q + 1)
            for c2 in range(CT):
                q_part(0, c2, c2 + 1)

            def phase(k, half, later, prep, last):
                f = 2 * k + half
                for t in range(GT):
                    n = GT * f + t
                    if t == 1 and later:
                        y_parts(f - 2)
                    if t < 2 and not (last and half):
                        q_part(1 - half, t, 2 * f + 3 + t)
                    scores_of_tile = ps[:, S_BANK + 2 * (t % 2):S_BANK + 2 * (t % 2) + 2, :].rearrange("p a n -> p (a n)")
                    act.wait_ge(exp_bias_ready, n + 1)
                    act.activation(probs[:, t % 2, :], scores_of_tile, ACT.Exp, bias=exp_bias[:, t % 2:t % 2 + 1],
                                   scale=col(SCORE_COL), accum_out=row_sum[:, half, t:t + 1]).then_inc(probs_ready, 1)
                    if later or half or t >= 2:
                        act.wait_ge(probs_turned[t % 2], 16 * (GT * k + 2 * half + t // 2))
                    act.activation(probs_n[:, t % 2, 0, :], scores_of_tile, ACT.Exp,
                                   bias=exp_bias[:, t % 2:t % 2 + 1],
                                   scale=col(SCORE_COL)).then_inc(probs_high, 1)
                    if prep and not half and t == 2:
                        xt_quarter(XT_BANK, (((k // HEADS) + 1) % 2) * 2, k % HEADS, k + HEADS + 1)

            def pair(k, later, prep, last):
                phase(k, 0, later, prep, last)
                phase(k, 1, later, prep, last)

            pair(0, False, True, False)
            with act.Fori(1, PAIRS - HEADS) as k:
                pair(k, True, True, False)
            with act.Fori(PAIRS - HEADS, PAIRS - 1) as k:
                pair(k, True, False, False)
            pair(PAIRS - 1, True, False, True)
            f = 2 * PAIRS
            y_parts(f - 2)
            y_parts(f - 1)

        @block.vector
        def _(dve):
            chain = [0]

            def link(ins):
                chain[0] += 1
                ins.then_inc(dve_chain, 1)
                dve.wait_ge(dve_chain, chain[0])

            def keep(r, i, h, m):
                dve.wait_ge(w_turned, r + 1)
                dve.tensor_copy(w_turn[:, m, h].rearrange("p s c -> p (s c)"),
                                ps[:, 4 + r % 4, :]).then_inc(w_kept_dve, 1)

            def spread_max(i, base):
                dve.tensor_scalar(spread[:, i, :], ones[:], col(base), None, ALU.mult).then_inc(spread_ready, 1)

            def scale(i, base, bank):
                dve.wait_ge(spread_turned, i + 1)
                link(dve.tensor_reduce(col(base), ps[:, bank, 0:P], AX.X, ALU.max))
                link(dve.tensor_scalar(col(base), col(base), TINY, None, ALU.max))
                link(dve.tensor_scalar(col(base + 1).bitcast(U32), col(base).bitcast(U32), EXP_MASK, None,
                                       ALU.bitwise_and))
                link(dve.reciprocal(col(base + 2), col(base + 1)))
                return dve.tensor_scalar(col(base + 3), col(base + 2), TOP, None, ALU.mult)

            def image_max(b):
                dve.wait_ge(x_in[b], 16)
                return dve.tensor_reduce(img_max[:, b:b + 1], x_res[:, b * JT * C:(b + 1) * JT * C], AX.X,
                                         ALU.max, apply_absolute_value=True)

            dve.wait_ge(const_ready, 3)
            for h in range(HEADS):
                keep(2 * h + 1, h, h, 1)
            keep(2 * HEADS + 1, HEADS, 1, 2)
            keep(2 * HEADS + 3, HEADS + 1, 3, 2)
            all_heads = ps[:, 0:HEADS, :].rearrange("p h n -> p (h n)")
            dve.wait_ge(a_made, HEADS)
            link(dve.tensor_reduce(col(A0), all_heads, AX.X, ALU.max, apply_absolute_value=True))
            spread_max(0, A0)
            image_max(0)
            scale(0, A0, 4).then_inc(scale_ready, 1)
            image_max(1)
            dve.wait_ge(a_high, 1)
            dve.scalar_tensor_tensor(out=a_w[:, ASIZE:2 * ASIZE], in0=all_heads, scalar=col(A_SCALE),
                                     in1=a_w[:, 0:ASIZE], op0=ALU.mult, op1=ALU.subtract).then_inc(a_split, 1)
            image_max(2)
            dve.wait_ge(m_made, HEADS)
            link(dve.tensor_reduce(col(M0), all_heads, AX.X, ALU.max, apply_absolute_value=True))
            spread_max(1, M0)
            image_max(3)
            scale(1, M0, 5).then_inc(scale_ready, 1)
            image_max(4)
            dve.wait_ge(m_high, 1)
            dve.scalar_tensor_tensor(out=m_w[:, ASIZE:2 * ASIZE], in0=all_heads, scalar=col(M_SCALE),
                                     in1=m_w[:, 0:ASIZE], op0=ALU.mult, op1=ALU.subtract).then_inc(m_split, 1)
            for b in range(5, B - 1):
                image_max(b)
            link(image_max(B - 1))
            link(dve.tensor_reduce(col(X0), img_max[:], AX.X, ALU.max))
            spread_max(2, X0)
            scale(2, X0, 6).then_inc(scale_ready, 1)
            dve.wait_ge(scale_ready, 3)
            dve.tensor_scalar(stage0, x_res[:, 0:JT * C], col(X_SCALE), None, ALU.mult).then_inc(stage0_ready, 1)
            link(dve.tensor_scalar(col(SC_A), col(X0 + 1), SCORE, None, ALU.mult))
            link(dve.tensor_scalar(col(SC_B), col(SC_A), col(A0 + 1), None, ALU.mult))
            link(dve.tensor_scalar(col(SCORE_COL), col(SC_B), col(X0 + 1), None, ALU.mult))
            link(dve.tensor_scalar(col(NEG_SCORE), col(SCORE_COL), -1.0, None, ALU.mult))
            link(dve.tensor_scalar(col(RES_A), col(X0 + 1), RESULT, None, ALU.mult))
            link(dve.tensor_scalar(col(RES_COL), col(RES_A), col(M0 + 1), None, ALU.mult))

            def xt_quarter(bank, par, q, done):
                dve.wait_ge(xt_high, done)

                def part(i):
                    return x_turn[:, bass.ds(par + i, 1), :, bass.ds(q * QUARTER, QUARTER)].rearrange(
                        "p a c n -> p (a c) n")
                dve.scalar_tensor_tensor(out=part(1), in0=ps[:, bank, :].rearrange("p (c n) -> p c n", c=CT),
                                         scalar=1.0, in1=part(0), op0=ALU.mult,
                                         op1=ALU.subtract).then_inc(xt_split, 1)

            def q_part(half, c2, done):
                cut = slice(half * GROUP, (half + 1) * GROUP)
                dve.wait_ge(q_high, done)
                dve.scalar_tensor_tensor(out=q_t[:, 1, c2, cut], in0=ps[:, MISC_BANK, :], scalar=Q_DOWN,
                                         in1=q_t[:, 0, c2, cut], op0=ALU.mult,
                                         op1=ALU.subtract).then_inc(q_split, 1)

            def y_parts(g):
                for c in range(CT):
                    dve.wait_ge(y_high, 2 * g + c + 1)
                    dve.scalar_tensor_tensor(out=y_t[:, 1, c, :], in0=ps[:, Y_BANK + c, :], scalar=Y_DOWN,
                                             in1=y_t[:, 0, c, :], op0=ALU.mult,
                                             op1=ALU.subtract).then_inc(y_split, 1)

            def probs_part(parity, n):
                dve.wait_ge(probs_high, n + 1)
                dve.tensor_tensor(probs_n[:, parity, 1, :], probs[:, parity, :], probs_n[:, parity, 0, :],
                                  ALU.subtract).then_inc(probs_split, 1)

            def row_factors(g, par):
                dve.wait_ge(probs_ready, GT * (g + 1))
                dve.reciprocal(row_inv[:, par, :], row_sum[:, par, :]).then_inc(inv_ready, 1)
                dve.wait_ge(inv_ready, g + 1)
                dve.tensor_scalar(row_fac[:, par, :], row_inv[:, par, :], col(RES_COL), None,
                                  ALU.mult).then_inc(fac_ready, 1)

            def add_out(k_of, g, half, pair_):
                dve.wait_ge(out_made, 2 * g + pair_ + 1)
                dve.wait_ge(fac_ready, g + 1)
                dve.wait_ge(added, 1 + GT * g)
                for i in range(2):
                    t = 2 * pair_ + i
                    dst = x_res[:, bass.ds((k_of // HEADS) * (JT * C) + (half * GT + t) * C, C)]
                    dve.scalar_tensor_tensor(out=dst, in0=ps[:, MISC_BANK, i * C:(i + 1) * C],
                                             scalar=row_fac[:, half, t:t + 1], in1=dst, op0=ALU.mult,
                                             op1=ALU.add).then_inc(added, 1)

            for q in range(HEADS):
                xt_quarter(q, 0, q, q + 1)
            for c2 in range(CT):
                q_part(0, c2, c2 + 1)
            dve.wait_ge(bias_in, 16)
            img0 = x_res[:, 0:JT * C].rearrange("p (t c) -> p t c", c=C)
            dve.tensor_tensor(img0, img0, bias[:, None, :].to_broadcast([P, JT, C]), ALU.add).then_inc(added, 1)

            def phase(k, half, later, prep, last):
                f = 2 * k + half
                for t in range(GT):
                    n = GT * f + t
                    if t == 1 and later:
                        y_parts(f - 2)
                    if later or half or t:
                        probs_part((t + 1) % 2, n - 1)
                    dve.wait_ge(scores_made, n + 1)
                    dve.tensor_reduce(row_max[:, t % 2:t % 2 + 1],
                                      ps[:, S_BANK + 2 * (t % 2):S_BANK + 2 * (t % 2) + 2, :].rearrange(
                                          "p a n -> p (a n)"),
                                      AX.X, ALU.max).then_inc(max_ready, 1)
                    dve.wait_ge(max_ready, n + 1)
                    dve.tensor_scalar(exp_bias[:, t % 2:t % 2 + 1], row_max[:, t % 2:t % 2 + 1], col(NEG_SCORE),
                                      PROB_SHIFT, ALU.mult, ALU.add).then_inc(exp_bias_ready, 1)
                    if t == 1 and (later or half):
                        row_factors(f - 1, 1 - half)
                    if t < 2 and not (last and half):
                        q_part(1 - half, t, 2 * f + 3 + t)
                    if t >= 2 and later:
                        add_out(k - 1, f - 2, half, t - 2)
                    if prep and not half and t == 2:
                        xt_quarter(XT_BANK, (((k // HEADS) + 1) % 2) * 2, k % HEADS, k + HEADS + 1)

            def pair(k, later, prep, last):
                phase(k, 0, later, prep, last)
                phase(k, 1, later, prep, last)

            pair(0, False, True, False)
            with dve.Fori(1, PAIRS - HEADS) as k:
                pair(k, True, True, False)
            with dve.Fori(PAIRS - HEADS, PAIRS - 1) as k:
                pair(k, True, False, False)
            pair(PAIRS - 1, True, False, True)
            f = 2 * PAIRS
            probs_part(1, GT * f - 1)
            y_parts(f - 2)
            row_factors(f - 1, 1)
            add_out(PAIRS - 1, f - 2, 0, 0)
            add_out(PAIRS - 1, f - 2, 0, 1)
            y_parts(f - 1)
            add_out(PAIRS - 1, f - 1, 1, 0)
            add_out(PAIRS - 1, f - 1, 1, 1)

        @block.gpsimd
        def _(pool):
            pool.memset(ones[:], 1.0).then_inc(const_ready, 1)
            pool.memset(ident[:], 0.0).then_inc(const_ready, 1)
            pool.wait_ge(const_ready, 2)
            pool.affine_select(out=ident[:], in_=ident[:], compare_op=ALU.not_equal, fill=1.0, base=0,
                               pattern=[[-1, P]], channel_multiplier=1).then_inc(const_ready, 1)
            pool.wait_ge(stage0_ready, 1)
            for q in range(HEADS):
                cut = slice(q * QT_TILES * C, (q + 1) * QT_TILES * C)
                low = slice(XSIZE + cut.start, XSIZE + cut.stop)
                pool.tensor_copy(x_nat[:, cut], stage0[:, cut]).then_inc(xn_high, 1)
                pool.wait_ge(xn_high, q + 1)
                pool.tensor_tensor(x_nat[:, low], stage0[:, cut], x_nat[:, cut], ALU.subtract).then_inc(xn_split, 1)

            def prepare(k, later):
                size = QT_TILES * C
                src = x_res[:, bass.ds((k + HEADS) * size, size)]
                o = (((k // HEADS) + 1) % 2) * (2 * XSIZE) + (k % HEADS) * size
                pool.wait_ge(scale_ready, 3)
                pool.tensor_copy(raw[:], src).then_inc(raw_ready, 1)
                pool.wait_ge(x_turned, k + HEADS)
                pool.wait_ge(raw_ready, k + 1)
                pool.wait_ge(scale_ready, 3)
                pool.tensor_tensor(stage[:], raw[:], col(X_SCALE).to_broadcast([P, size]), ALU.mult).then_inc(stage_ready, 1)
                pool.wait_ge(bias_in, 16)
                pool.tensor_tensor(src.rearrange("p (t c) -> p t c", c=C), raw[:].rearrange("p (t c) -> p t c", c=C),
                                   bias[:, None, :].to_broadcast([P, QT_TILES, C]), ALU.add).then_inc(pool_chain, 1)
                pool.wait_ge(stage_ready, k + 1)
                if later:
                    pool.wait_ge(y_made, 4 * k)
                pool.wait_ge(scale_ready, 3)
                pool.tensor_copy(x_nat[:, bass.ds(o, size)], stage[:]).then_inc(xn_high, 1)
                pool.wait_ge(pool_chain, k + 1)
                pool.wait_ge(xn_high, k + HEADS + 1)
                pool.wait_ge(scale_ready, 3)
                pool.tensor_tensor(x_nat[:, bass.ds(o + XSIZE, size)], stage[:], x_nat[:, bass.ds(o, size)],
                                   ALU.subtract).then_inc(xn_split, 1)
                pool.wait_ge(xn_split, k + HEADS + 1)

            prepare(0, False)
            with pool.Fori(1, PAIRS - HEADS) as k:
                prepare(k, True)


_INS = ['x', 'L0_conv_W_qkv', 'L0_conv_W_out', 'L0_conv_b_out']
_OUTS = [((8, 32, 32, 256), 'float32')]


def kernel(**inputs):
    import numpy as _np
    import concourse.bacc as _bacc
    from concourse import mybir as _mybir
    from concourse.bass_utils import run_bass_kernel_spmd as _run

    nc = _bacc.Bacc("TRN2", target_bir_lowering=False, num_devices=1)
    arrays, args = {}, []
    for name in _INS:
        a = _np.ascontiguousarray(inputs[name])
        arrays[f"in_{name}_dram"] = a
        args.append(nc.dram_tensor(f"in_{name}_dram", a.shape, _mybir.dt.from_np(a.dtype), kind="ExternalInput").ap())
    for i, (shape, dtype) in enumerate(_OUTS):
        dt = _mybir.dt.from_np(_np.dtype(dtype))
        args.append(nc.dram_tensor(f"out_{i}_dram", shape, dt, kind="ExternalOutput").ap())
    attention(nc, *args)
    r = _run(nc, [arrays], core_ids=[0])
    got = tuple(r.results[0][f"out_{i}_dram"] for i in range(len(_OUTS)))
    return got[0]
```

```python
from contextlib import ExitStack

import concourse.bass as bass
from concourse import mybir

ALU = mybir.AluOpType
ACT = mybir.ActivationFunctionType
AX = mybir.AxisListType
F32 = mybir.dt.float32
F16 = mybir.dt.float16
U32 = mybir.dt.uint32

P = 128
BANK = 512

S_BANK = 0
Y_BANK = 4
MISC_BANK = 6
XT_BANK = 7
PREV_BANKS = (0, 1, 6, 7)
LAST_BANKS = (2, 3, 6, 7)

TOP = 2.0 ** 14
TINY = 2.0 ** -80
EXP_MASK = 0x7F800000
LN2 = 0.6931471805599453
PROB_SHIFT = 14 * LN2


def attention(nc, x, w_qkv, w_out, b_out, out):
    B, H, W, C = x.shape
    N = H * W
    HEADS = w_out.shape[0] // C
    CT = C // P
    JT = N // P
    PAIRS = B * HEADS
    GROUP = N // 2
    GT = GROUP // P
    QUARTER = N // HEADS
    QT_TILES = QUARTER // P
    assert C == 2 * P and HEADS == 4 and N == 2 * BANK and GT == 4 and QT_TILES == 2

    Q_DOWN = 1.0 / (4 * C * TOP)
    Y_DOWN = 1.0 / (N * TOP)
    SCORE = C ** -0.5 / (Q_DOWN * TOP ** 3)
    RESULT = 1.0 / (Y_DOWN * TOP ** 2)

    with ExitStack() as ctx:
        def sb(name, shape, dt):
            return ctx.enter_context(nc.sbuf_tensor(name, shape, dt))

        def sem(name):
            return ctx.enter_context(nc.semaphore(name))

        XSIZE = CT * N
        ASIZE = HEADS * CT * C
        TILE = 2 * N
        x_res = sb("x_res", [P, B * JT * C], F32)
        x_nat = sb("x_nat", [P, 4 * XSIZE], F16)
        x_turn = sb("x_turn", [P, 4, CT, N], F16)
        probs = sb("probs", [P, 2, N], F32)
        probs_t = sb("probs_t", [P, 2, 2, JT, GROUP], F16)
        q_t = sb("q_t", [P, 2, CT, N], F16)
        y_t = sb("y_t", [P, 2, CT, GROUP], F16)
        a_w = sb("a_w", [P, 2 * ASIZE], F16)
        m_w = sb("m_w", [P, 2 * ASIZE], F16)
        wqk = sb("wqk", [P, CT, HEADS, 2 * C], F32)
        wv = sb("wv", [P, CT, HEADS, C], F32)
        wo = sb("wo", [P, HEADS * CT, C], F32)
        wqk_flat = wqk[:].rearrange("p s h n -> p (s h n)")
        probs_n = wqk_flat.bitcast(F16)[:, 0:2 * TILE].rearrange("p (a i n) -> p a i n", a=2, i=2)
        m_raw = wqk_flat[:, TILE:TILE + ASIZE]
        bias = sb("bias", [P, C], F32)
        stage = sb("stage", [P, QT_TILES * C], F32)
        raw = sb("raw", [P, QT_TILES * C], F32)
        ident = sb("ident", [P, P], F32)
        ones = sb("ones", [P, P], F32)
        spread = sb("spread", [P, 4, P], F32)
        img_max = sb("img_max", [P, B], F32)
        head_max = sb("head_max", [P, HEADS], F32)
        cols = sb("cols", [P, 32], F32)
        x_scale = sb("x_scale", [P, B], F32)
        score_scale = sb("score_scale", [P, B], F32)
        neg_scale = sb("neg_scale", [P, B], F32)
        x_power = sb("x_power", [P, B], F32)
        res_scale = sb("res_scale", [P, B], F32)
        res_m = sb("res_m", [P, 1], F32)
        pool_scale = sb("pool_scale", [P, 1], F32)
        exp_scale = sb("exp_scale", [P, 2], F32)
        row_max = sb("row_max", [P, 2], F32)
        exp_bias = sb("exp_bias", [P, 2], F32)
        row_sum = sb("row_sum", [P, 2, GT], F32)
        row_inv = sb("row_inv", [P, 2, GT], F32)
        row_fac = sb("row_fac", [P, 2, GT], F32)
        ps = ctx.enter_context(nc.psum_tensor("ps", [P, 8, BANK], F32))

        pt32 = probs_t[:].rearrange("p a b j i -> p (a b j i)").bitcast(F32)
        w_turn = pt32[:, 0:3 * HEADS * CT * C].rearrange("p (m h s c) -> p m h s c", m=3, h=HEADS, s=CT)
        stage0 = pt32[:, 3 * HEADS * CT * C:3 * HEADS * CT * C + JT * C]

        def col(i):
            return cols[:, i:i + 1]
        A0, M0, XF0, XO0, TMP = 0, 4, 8, 12, 16
        A_SCALE, M_SCALE = A0 + 3, M0 + 3
        FIRST = 2

        w_in = [sem(f"w_in{h}") for h in range(HEADS)]
        wv_in = sem("wv_in")
        x_in = [sem(f"x_in{b}") for b in range(B)]
        wo_in, bias_in, stored = sem("wo_in"), sem("bias_in"), sem("stored")
        const_ready = sem("const_ready")
        w_kept_act, w_kept_dve = sem("w_kept_act"), sem("w_kept_dve")
        a_made, m_made = sem("a_made"), sem("m_made")
        a_high, a_split = sem("a_high"), sem("a_split")
        m_kept, m_high, m_split = sem("m_kept"), sem("m_high"), sem("m_split")
        m_scaled_ready = sem("m_scaled_ready")
        wv_turned, wv_kept = sem("wv_turned"), sem("wv_kept")
        spread_ready, spread_turned = sem("spread_ready"), sem("spread_turned")
        a_scale_ready, m_scale_ready = sem("a_scale_ready"), sem("m_scale_ready")
        res_ready = sem("res_ready")
        x_scale_ready = sem("x_scale_ready")
        pool_scale_ready = sem("pool_scale_ready")
        stage0_ready = sem("stage0_ready")
        dve_chain = sem("dve_chain")
        scores_made = sem("scores_made")
        y_made = sem("y_made")
        q_made = sem("q_made")
        out_made = sem("out_made")
        x_turned = sem("x_turned")
        probs_ready = sem("probs_ready")
        probs_high = sem("probs_high")
        y_high = sem("y_high")
        q_high = sem("q_high")
        xt_high = sem("xt_high")
        max_ready = sem("max_ready")
        exp_bias_ready = sem("exp_bias_ready")
        probs_split = sem("probs_split")
        y_split = sem("y_split")
        q_split = sem("q_split")
        xt_split = sem("xt_split")
        inv_ready = sem("inv_ready")
        fac_ready = sem("fac_ready")
        added = sem("added")
        probs_turned = [sem(f"probs_turned{i}") for i in range(2)]
        stage_ready = sem("stage_ready")
        raw_ready = sem("raw_ready")
        bias_given = sem("bias_given")
        xn_high = sem("xn_high")
        xn_split = sem("xn_split")
        turns_begun = sem("turns_begun")
        w_turned = sem("w_turned")

        x_dram = x.rearrange("b h w c -> (b h w) c").rearrange("(b t p) c -> b p t c", b=B, p=P)
        out_dram = out.rearrange("b h w c -> (b h w) c").rearrange("(g t p) c -> g p t c", g=2 * B, p=P)

        block = ctx.enter_context(nc.Block())

        @block.sync
        def _(sp):
            wsrc = w_qkv.rearrange("(s p) (h n) -> p s h n", p=P, h=HEADS)

            def load_image(b):
                dst = x_res[:, b * JT * C:(b + 1) * JT * C].rearrange("p (t c) -> p t c", c=C)
                sp.dma_start(dst, x_dram[b]).then_inc(x_in[b], 16)

            for h in range(HEADS):
                sp.dma_start(wqk[:, :, h, :], wsrc[:, :, h, 0:2 * C]).then_inc(w_in[h], 16)
                if h % 2:
                    load_image(h // 2)
            for s in range(CT):
                sp.dma_start(wv[:, s], wsrc[:, s, :, 2 * C:3 * C]).then_inc(wv_in, 16)
            sp.dma_start(wo[:], w_out.rearrange("(s p) c -> p s c", p=P)).then_inc(wo_in, 16)
            sp.dma_start(bias[:], b_out.rearrange("(a c) -> a c", a=1).broadcast_to([P, C])).then_inc(bias_in, 16)
            for b in range(FIRST, B):
                load_image(b)

            def turn_tile(k, half, t, later):
                f, parity = 2 * k + half, t % 2
                sp.wait_ge(probs_split, GT * f + t + 1)
                if t == 0 and later:
                    sp.wait_ge(y_made, 2 * (f - 2) + 2)
                sp.sem_inc(turns_begun, 1)
                dst = probs_t[:, half].rearrange("p i j q -> p (i j) q")[:, :, t * P:(t + 1) * P]
                src = probs_n[:, parity].rearrange("p i n -> p (i n)")
                sp.dma_start_transpose(dst, src).then_inc(probs_turned[parity], 16)

            def turn_pair(k, later):
                for half in range(2):
                    if half and not later:
                        sp.wait_ge(xn_split, HEADS)
                        sp.wait_ge(m_made, HEADS)
                    for t in range(GT):
                        turn_tile(k, half, t, later)

            def store(b, half):
                sp.wait_ge(added, 1 + GT * (2 * HEADS * b + 2 * HEADS - 1 + half))
                src = x_res[:, bass.ds((b * 2 + half) * GT * C, GT * C)].rearrange("p (t c) -> p t c", c=C)
                dst = out_dram[bass.ds(b * 2 + half, 1)].rearrange("g p t c -> p (g t) c")
                sp.dma_start(dst, src).then_inc(stored, 16)

            for h in range(HEADS):
                turn_pair(h, h > 0)
            with sp.Fori(1, B) as b:
                for h in range(HEADS):
                    turn_pair(HEADS * b + h, True)
                    if h == 1:
                        store(b - 1, 0)
                        store(b - 1, 1)
            store(B - 1, 0)
            store(B - 1, 1)
            sp.wait_ge(stored, 16 * 2 * B)

        @block.tensor
        def _(pe):
            def turn_weights(r, h, m):
                if r >= 4:
                    if r % 2 == 0:
                        pe.wait_ge(w_kept_act, (r - 4) // 2 + 1)
                    else:
                        pe.wait_ge(w_kept_dve, (r - 4) // 2 + 1)
                for s in range(CT):
                    for c in range(CT):
                        mm = pe.transpose(ps[:, 4 + r % 4, s * C + c * P:s * C + (c + 1) * P],
                                          wqk[:, c, h, m * C + s * P:m * C + (s + 1) * P], ident[:])
                mm.then_inc(w_turned, 1)

            def turn_v(h):
                if h == 0:
                    pe.wait_ge(wv_in, 16 * CT)
                    pe.wait_ge(q_split, CT)
                else:
                    pe.wait_ge(wv_kept, h)
                for s in range(CT):
                    for c in range(CT):
                        mm = pe.transpose(ps[:, XT_BANK, s * C + c * P:s * C + (c + 1) * P],
                                          wv[:, c, h, s * P:(s + 1) * P], ident[:])
                mm.then_inc(wv_turned, 1)

            def turn_column(i, bank):
                pe.wait_ge(spread_ready, i + 1)
                pe.transpose(ps[:, bank, 0:P], spread[:, i, :], ident[:]).then_inc(spread_turned, 1)

            def m_product(h):
                if h == 0:
                    pe.wait_ge(wo_in, 16)
                    pe.wait_ge(xt_split, HEADS)
                elif h >= 2:
                    pe.wait_ge(m_kept, h - 1)
                pe.wait_ge(wv_kept, h + 1)
                product(Y_BANK + h % 2, w_turn[:, 2, h], wo[:, h * CT:(h + 1) * CT, :], m_made)

            def product(bank, left, right, done):
                for c in range(CT):
                    for s in range(CT):
                        mm = pe.matmul(ps[:, bank, c * C:(c + 1) * C], left[:, s, c * P:(c + 1) * P],
                                       right[:, s, :], start=(s == 0), stop=(s == CT - 1))
                mm.then_inc(done, 1)

            pe.wait_ge(const_ready, 3)
            for h in range(HEADS + 1):
                if h < HEADS:
                    pe.wait_ge(w_in[h], 16)
                    turn_weights(2 * h, h, 0)
                    turn_weights(2 * h + 1, h, 1)
                if h >= 1:
                    pe.wait_ge(w_kept_act, h)
                    pe.wait_ge(w_kept_dve, h)
                    product(h - 1, w_turn[:, 0, h - 1], w_turn[:, 1, h - 1], a_made)
            turn_column(0, 4)
            turn_column(1, 5)
            pe.wait_ge(stage0_ready, 1)
            for q in range(HEADS):
                if q == 1:
                    pe.wait_ge(a_scale_ready, 1)
                for c in range(CT):
                    for j in range(QT_TILES):
                        o = (q * QT_TILES + j) * C + c * P
                        mm = pe.transpose(ps[:, 4 + q, c * QUARTER + j * P:c * QUARTER + (j + 1) * P],
                                          stage0[:, o:o + P], ident[:])
                mm.then_inc(x_turned, 1)

            def parts():
                return ((0, 0), (0, 1), (1, 0))

            def q_bank(k_of, half, c2, bank=MISC_BANK):
                head = (k_of % HEADS) * (CT * C)
                par = ((k_of // HEADS) % 2) * 2
                first = True
                for c in range(CT):
                    for l, r in parts():
                        lhs = a_w[:, bass.ds(head + (l * ASIZE + c * C + c2 * P), P)]
                        rhs = x_turn[:].rearrange("p a c n -> p (a c n)")[
                            :, bass.ds(par * (CT * N) + ((r * CT + c) * N + half * GROUP), GROUP)]
                        mm = pe.matmul(ps[:, bank, :], lhs, rhs, start=first,
                                       stop=(c == CT - 1 and (l, r) == (1, 0)))
                        first = False
                mm.then_inc(q_made, 1)

            def out_bank(k_of, pair):
                head = (k_of % HEADS) * (CT * C)
                for i in range(2):
                    q0 = (2 * pair + i) * P
                    first = True
                    for c in range(CT):
                        for l, r in parts():
                            mm = pe.matmul(ps[:, MISC_BANK, i * C:(i + 1) * C], y_t[:, l, c, q0:q0 + P],
                                           m_w[:, bass.ds(head + (r * ASIZE + c * C), C)],
                                           start=first, stop=(c == CT - 1 and (l, r) == (1, 0)))
                            first = False
                mm.then_inc(out_made, 1)

            def last_out(q, bank, c):
                for l, r in parts():
                    o = r * ASIZE + ((HEADS - 1) * CT + c) * C
                    mm = pe.matmul(ps[:, bank, 0:C], y_t[:, l, c, q * P:(q + 1) * P], m_w[:, o:o + C],
                                   start=(c == 0 and (l, r) == (0, 0)),
                                   stop=(c == CT - 1 and (l, r) == (1, 0)))
                if c == CT - 1 and q % 2:
                    mm.then_inc(out_made, 1)

            def scores(k, half, t):
                par = ((k // HEADS) % 2) * 2
                q0 = half * GROUP + t * P
                for j in range(2):
                    first = True
                    for c in range(CT):
                        for l, r in parts():
                            rhs = x_turn[:].rearrange("p a c n -> p (a c n)")[
                                :, bass.ds(par * (CT * N) + ((r * CT + c) * N + j * BANK), BANK)]
                            mm = pe.matmul(ps[:, S_BANK + 2 * (t % 2) + j, :], q_t[:, l, c, q0:q0 + P], rhs,
                                           start=first, stop=(c == CT - 1 and (l, r) == (1, 0)))
                            first = False
                mm.then_inc(scores_made, 1)

            def weigh(k_of, par_group, t, c):
                img = ((k_of // HEADS) % 2) * (2 * XSIZE)
                for j in (2 * t, 2 * t + 1):
                    for l, r in parts():
                        lhs = x_nat[:, bass.ds(img + (l * XSIZE + j * C + c * P), P)]
                        mm = pe.matmul(ps[:, Y_BANK + c, :], lhs, probs_t[:, par_group, r, j, :],
                                       start=(j == 0 and (l, r) == (0, 0)),
                                       stop=(j == JT - 1 and (l, r) == (1, 0)))
                return mm

            pe.wait_ge(a_split, 1)
            for c2 in range(CT):
                pe.wait_ge(xt_split, 3 + c2)
                q_bank(0, 0, c2, MISC_BANK + c2)

            def phase(k, half, later, prep, last):
                f = 2 * k + half
                for t in range(GT):
                    n = GT * f + t
                    if not later and n < HEADS:
                        turn_v(n)
                    if not later and half and t == 3:
                        pe.wait_ge(q_split, 2 * f + 4)
                        turn_column(2, MISC_BANK)
                    if not later and n < 2:
                        pe.wait_ge(a_split, 2 * n + 2)
                    if t == 0:
                        pe.wait_ge(q_split, 2 * f + 2)
                        pe.wait_ge(xt_split, HEADS * (k // HEADS) + 4)
                    if later or half or t >= 2:
                        pe.wait_ge(probs_high, n - 1)
                    scores(k, half, t)
                    if t < 2 and not (last and half):
                        if t == 0 and later:
                            pe.wait_ge(added, 1 + GT * (f - 2))
                        if t == 0 and later and not half:
                            pe.wait_ge(m_scale_ready, 1)
                        if t == 1:
                            pe.wait_ge(q_split, 2 * f + 3)
                        if t == 0 and half:
                            pe.wait_ge(xt_split, HEADS * ((k + 1) // HEADS) + 2)
                        q_bank(k + half, 1 - half, t)
                    if t >= 2 and later:
                        if t == 2:
                            if last and half:
                                pe.wait_ge(added, 1 + GT * (f - 2))
                            else:
                                pe.wait_ge(q_split, 2 * f + 4)
                            pe.wait_ge(y_split, 2 * (f - 2) + 2)
                            pe.wait_ge(m_split, 1)
                        if t == 3:
                            pe.wait_ge(added, 1 + GT * (f - 2) + 2)
                        out_bank(k - 1, t - 2)
                    if not later and 1 <= n <= HEADS:
                        m_product(n - 1)
                    if prep and half and t == 2:
                        pe.wait_ge(stage_ready, k + 1)
                        pe.wait_ge(xt_split, k + HEADS)
                        if later:
                            pe.wait_ge(x_scale_ready, 2)
                        else:
                            pe.wait_ge(wv_kept, HEADS)
                        for c in range(CT):
                            for j in range(QT_TILES):
                                mm = pe.transpose(ps[:, XT_BANK, c * QUARTER + j * P:c * QUARTER + (j + 1) * P],
                                                  stage[:, j * C + c * P:j * C + (c + 1) * P], ident[:])
                        mm.then_inc(x_turned, 1)
                    if t == 0 and later:
                        for c in range(CT):
                            weigh(k - 1, half, GT - 1, c).then_inc(y_made, 1)
                    if t >= 1 and (later or half):
                        k_of = k if half else k - 1
                        if t == 1:
                            pe.wait_ge(probs_turned[0], 32 * f)
                            pe.wait_ge(probs_turned[1], 32 * f)
                            pe.wait_ge(xn_split, HEADS * (k_of // HEADS) + 4)
                        for c in range(CT):
                            if t == 1:
                                if later:
                                    pe.wait_ge(y_split, 2 * (f - 2) + c + 1)
                                else:
                                    pe.wait_ge(m_kept, HEADS - 1 + c)
                            weigh(k_of, 1 - half, t - 1, c)
                    if not later and half and t == 3:
                        pe.wait_ge(xt_split, HEADS + 1)
                        turn_column(3, XT_BANK)

            def pair(k, later, prep, last):
                phase(k, 0, later, prep, last)
                phase(k, 1, later, prep, last)

            pair(0, False, True, False)
            with pe.Fori(1, PAIRS - HEADS) as k:
                pair(k, True, True, False)
            with pe.Fori(PAIRS - HEADS, PAIRS - 1) as k:
                pair(k, True, False, False)
            pair(PAIRS - 1, True, False, True)

            f = 2 * PAIRS
            for c in range(CT):
                weigh(PAIRS - 1, 0, GT - 1, c).then_inc(y_made, 1)
            pe.wait_ge(probs_high, GT * f - 1)
            pe.wait_ge(added, 1 + GT * (f - 2))
            for c in range(CT):
                pe.wait_ge(y_split, 2 * (f - 2) + c + 1)
                for q in range(GT):
                    last_out(q, PREV_BANKS[q], c)
            pe.wait_ge(probs_turned[0], 32 * f)
            pe.wait_ge(probs_turned[1], 32 * f)
            pe.wait_ge(probs_high, GT * f)
            for c in range(CT):
                for t in range(GT):
                    mm = weigh(PAIRS - 1, 1, t, c)
                mm.then_inc(y_made, 1)
            pe.wait_ge(added, 1 + GT * (f - 1))
            for c in range(CT):
                pe.wait_ge(y_split, 2 * (f - 1) + c + 1)
                for q in range(GT):
                    last_out(q, LAST_BANKS[q], c)

        @block.scalar
        def _(act):
            def keep(r, h):
                act.wait_ge(w_turned, r + 1)
                act.activation(w_turn[:, 0, h].rearrange("p s c -> p (s c)"), ps[:, 4 + r % 4, :],
                               ACT.Copy).then_inc(w_kept_act, 1)

            for h in range(HEADS):
                keep(2 * h, h)
            act.wait_ge(a_scale_ready, 1)

            def a_part(h):
                act.activation(a_w[:, h * CT * C:(h + 1) * CT * C], ps[:, h, :], ACT.Copy,
                               scale=col(A_SCALE)).then_inc(a_high, 1)

            a_part(0)
            a_part(1)

            def xt_quarter(bank, par, q, done):
                act.wait_ge(x_turned, done)
                act.activation(x_turn[:, bass.ds(par, 1), :, bass.ds(q * QUARTER, QUARTER)].rearrange(
                    "p a c n -> p (a c) n"), ps[:, bank, :].rearrange("p (c n) -> p c n", c=CT),
                    ACT.Copy).then_inc(xt_high, 1)

            def q_part(half, c2, done, bank=MISC_BANK):
                act.wait_ge(q_made, done)
                act.activation(q_t[:, 0, c2, half * GROUP:(half + 1) * GROUP], ps[:, bank, :],
                               ACT.Copy, scale=Q_DOWN).then_inc(q_high, 1)

            def y_parts(g):
                for c in range(CT):
                    act.wait_ge(y_made, 2 * g + c + 1)
                    act.activation(y_t[:, 0, c, :], ps[:, Y_BANK + c, :], ACT.Copy,
                                   scale=Y_DOWN).then_inc(y_high, 1)

            for q in range(HEADS):
                xt_quarter(4 + q, 0, q, q + 1)
            for c2 in range(CT):
                q_part(0, c2, c2 + 1, MISC_BANK + c2)
                a_part(2 + c2)

            def phase(k, half, later, prep, last):
                f = 2 * k + half
                for t in range(GT):
                    n = GT * f + t
                    if not later and n < HEADS:
                        act.wait_ge(wv_turned, n + 1)
                        act.activation(w_turn[:, 2, n].rearrange("p s c -> p (s c)"), ps[:, XT_BANK, :],
                                       ACT.Copy).then_inc(wv_kept, 1)
                    if not later and 2 <= n <= HEADS + 1:
                        act.wait_ge(m_made, n - 1)
                        act.activation(m_raw[:, (n - 2) * CT * C:(n - 1) * CT * C], ps[:, Y_BANK + n % 2, :],
                                       ACT.Copy).then_inc(m_kept, 1)
                    if t == 1 and later:
                        y_parts(f - 2)
                    if t < 2 and not (last and half):
                        q_part(1 - half, t, 2 * f + 3 + t)
                    banks = slice(S_BANK + 2 * (t % 2), S_BANK + 2 * (t % 2) + 2)
                    scores_of_tile = ps[:, banks, :].rearrange("p a n -> p (a n)")
                    act.wait_ge(exp_bias_ready, n + 1)
                    act.activation(probs[:, t % 2, :], scores_of_tile, ACT.Exp, bias=exp_bias[:, t % 2:t % 2 + 1],
                                   scale=exp_scale[:, half:half + 1],
                                   accum_out=row_sum[:, half, t:t + 1]).then_inc(probs_ready, 1)
                    if later or half or t >= 2:
                        act.wait_ge(probs_turned[t % 2], 16 * (GT * k + 2 * half + t // 2))
                    act.activation(probs_n[:, t % 2, 0, :], scores_of_tile, ACT.Exp,
                                   bias=exp_bias[:, t % 2:t % 2 + 1],
                                   scale=exp_scale[:, half:half + 1]).then_inc(probs_high, 1)
                    if prep and half and t == 2:
                        xt_quarter(XT_BANK, (((k // HEADS) + 1) % 2) * 2, k % HEADS, k + HEADS + 1)

            def pair(k, later, prep, last):
                phase(k, 0, later, prep, last)
                phase(k, 1, later, prep, last)

            pair(0, False, True, False)
            act.wait_ge(m_scale_ready, 1)
            act.activation(m_w[:, 0:ASIZE], m_raw, ACT.Copy, scale=col(M_SCALE)).then_inc(m_high, 1)
            with act.Fori(1, PAIRS - HEADS) as k:
                pair(k, True, True, False)
            with act.Fori(PAIRS - HEADS, PAIRS - 1) as k:
                pair(k, True, False, False)
            pair(PAIRS - 1, True, False, True)
            f = 2 * PAIRS
            y_parts(f - 2)
            y_parts(f - 1)

        @block.vector
        def _(dve):
            chain = [0]

            def link(ins):
                chain[0] += 1
                ins.then_inc(dve_chain, 1)
                dve.wait_ge(dve_chain, chain[0])

            def keep(r, h):
                dve.wait_ge(w_turned, r + 1)
                dve.tensor_copy(w_turn[:, 1, h].rearrange("p s c -> p (s c)"),
                                ps[:, 4 + r % 4, :]).then_inc(w_kept_dve, 1)

            def spread_max(i, base):
                dve.tensor_scalar(spread[:, i, :], ones[:], col(base), None, ALU.mult).then_inc(spread_ready, 1)

            def scale(i, base, bank):
                dve.wait_ge(spread_turned, i + 1)
                link(dve.tensor_reduce(col(base), ps[:, bank, 0:P], AX.X, ALU.max))
                link(dve.tensor_scalar(col(base), col(base), TINY, None, ALU.max))
                link(dve.tensor_scalar(col(base + 1).bitcast(U32), col(base).bitcast(U32), EXP_MASK, None,
                                       ALU.bitwise_and))
                link(dve.reciprocal(col(base + 2), col(base + 1)))
                return dve.tensor_scalar(col(base + 3), col(base + 2), TOP, None, ALU.mult)

            def tables(base, first, end):
                def fill(table, value, times=None):
                    return dve.tensor_scalar(table[:, first:end], ones[:, first:end], value, times,
                                             ALU.mult, *(() if times is None else (ALU.mult,)))
                link(dve.tensor_scalar(col(TMP), col(base + 1), SCORE, col(A0 + 1), ALU.mult, ALU.mult))
                link(dve.tensor_scalar(col(TMP + 1), col(TMP), col(base + 1), None, ALU.mult))
                fill(score_scale, col(TMP + 1))
                fill(neg_scale, col(TMP + 1), -1.0)
                link(fill(x_power, col(base + 1)))

            def image_max(b):
                dve.wait_ge(x_in[b], 16)
                return dve.tensor_reduce(img_max[:, b:b + 1], x_res[:, b * JT * C:(b + 1) * JT * C], AX.X,
                                         ALU.max, apply_absolute_value=True)

            def a_max(h):
                dve.wait_ge(a_made, h + 1)
                return dve.tensor_reduce(head_max[:, h:h + 1], ps[:, h, :], AX.X, ALU.max,
                                         apply_absolute_value=True)

            def a_part(h):
                o = h * CT * C
                dve.wait_ge(a_high, h + 1)
                dve.scalar_tensor_tensor(out=a_w[:, ASIZE + o:ASIZE + o + CT * C], in0=ps[:, h, :],
                                         scalar=col(A_SCALE), in1=a_w[:, o:o + CT * C], op0=ALU.mult,
                                         op1=ALU.subtract).then_inc(a_split, 1)

            dve.wait_ge(const_ready, 3)
            for h in range(HEADS):
                keep(2 * h + 1, h)
                if h >= 1:
                    a_max(h - 1)
                if h == 1:
                    image_max(0)
            link(image_max(1))
            link(dve.tensor_reduce(col(XF0), img_max[:, 0:FIRST], AX.X, ALU.max))
            spread_max(0, XF0)
            link(a_max(HEADS - 1))
            link(dve.tensor_reduce(col(A0), head_max[:], AX.X, ALU.max))
            spread_max(1, A0)
            link(scale(0, XF0, 4))
            dve.tensor_scalar(stage0, x_res[:, 0:JT * C], col(XF0 + 3), None, ALU.mult).then_inc(stage0_ready, 1)
            scale(1, A0, 5).then_inc(a_scale_ready, 1)
            a_part(0)
            a_part(1)

            def xt_quarter(bank, par, q, done):
                dve.wait_ge(xt_high, done)

                def part(i):
                    return x_turn[:, bass.ds(par + i, 1), :, bass.ds(q * QUARTER, QUARTER)].rearrange(
                        "p a c n -> p (a c) n")
                dve.scalar_tensor_tensor(out=part(1), in0=ps[:, bank, :].rearrange("p (c n) -> p c n", c=CT),
                                         scalar=1.0, in1=part(0), op0=ALU.mult,
                                         op1=ALU.subtract).then_inc(xt_split, 1)

            def q_part(half, c2, done, bank=MISC_BANK):
                cut = slice(half * GROUP, (half + 1) * GROUP)
                dve.wait_ge(q_high, done)
                dve.scalar_tensor_tensor(out=q_t[:, 1, c2, cut], in0=ps[:, bank, :], scalar=Q_DOWN,
                                         in1=q_t[:, 0, c2, cut], op0=ALU.mult,
                                         op1=ALU.subtract).then_inc(q_split, 1)

            def y_parts(g):
                for c in range(CT):
                    dve.wait_ge(y_high, 2 * g + c + 1)
                    dve.scalar_tensor_tensor(out=y_t[:, 1, c, :], in0=ps[:, Y_BANK + c, :], scalar=Y_DOWN,
                                             in1=y_t[:, 0, c, :], op0=ALU.mult,
                                             op1=ALU.subtract).then_inc(y_split, 1)

            def probs_part(parity, n):
                dve.wait_ge(probs_high, n + 1)
                dve.tensor_tensor(probs_n[:, parity, 1, :], probs[:, parity, :], probs_n[:, parity, 0, :],
                                  ALU.subtract).then_inc(probs_split, 1)

            def row_factors(k_of, g, par):
                dve.wait_ge(probs_ready, GT * (g + 1))
                dve.reciprocal(row_inv[:, par, :], row_sum[:, par, :]).then_inc(inv_ready, 1)
                dve.wait_ge(inv_ready, g + 1)
                dve.tensor_scalar(row_fac[:, par, :], row_inv[:, par, :],
                                  res_scale[:, bass.ds(k_of // HEADS, 1)], None,
                                  ALU.mult).then_inc(fac_ready, 1)

            def add_out(k_of, g, half, pair_):
                dve.wait_ge(out_made, 2 * g + pair_ + 1)
                dve.wait_ge(fac_ready, g + 1)
                dve.wait_ge(added, 1 + GT * g)
                for i in range(2):
                    t = 2 * pair_ + i
                    dst = x_res[:, bass.ds((k_of // HEADS) * (JT * C) + (half * GT + t) * C, C)]
                    dve.scalar_tensor_tensor(out=dst, in0=ps[:, MISC_BANK, i * C:(i + 1) * C],
                                             scalar=row_fac[:, half, t:t + 1], in1=dst, op0=ALU.mult,
                                             op1=ALU.add).then_inc(added, 1)

            for q in range(HEADS):
                xt_quarter(4 + q, 0, q, q + 1)
            for c2 in range(CT):
                q_part(0, c2, c2 + 1, MISC_BANK + c2)
            a_part(2)
            a_part(3)
            tables(XF0, 0, FIRST)
            dve.tensor_copy(x_scale[:, 0:FIRST], col(XF0 + 3).to_broadcast([P, FIRST])).then_inc(x_scale_ready, 1)

            def extras(n):
                if n <= 4:
                    image_max(FIRST + n)
                elif n == 5:
                    dve.wait_ge(m_kept, HEADS)
                    link(dve.tensor_reduce(col(M0), m_raw, AX.X, ALU.max, apply_absolute_value=True))
                    spread_max(2, M0)
                elif n == 6:
                    link(image_max(B - 1))
                    link(dve.tensor_reduce(col(XO0), img_max[:, FIRST:B], AX.X, ALU.max))
                    spread_max(3, XO0)
                else:
                    link(scale(2, M0, MISC_BANK))
                    dve.tensor_scalar(res_m[:], col(M0 + 1), RESULT, None, ALU.mult).then_inc(m_scale_ready, 1)
                    dve.wait_ge(m_scale_ready, 1)
                    dve.tensor_scalar(res_scale[:, 0:FIRST], x_power[:, 0:FIRST], res_m[:], None,
                                      ALU.mult).then_inc(res_ready, 1)
                    dve.wait_ge(res_ready, 1)
                    row_factors(0, 0, 0)

            def finish_start():
                link(scale(3, XO0, XT_BANK))
                tables(XO0, FIRST, B)
                link(dve.tensor_copy(x_scale[:, FIRST:B], col(XO0 + 3).to_broadcast([P, B - FIRST])))
                dve.tensor_scalar(res_scale[:, FIRST:B], x_power[:, FIRST:B], res_m[:], None,
                                  ALU.mult).then_inc(x_scale_ready, 1)

            def phase(k, half, later, prep, last):
                f = 2 * k + half
                for t in range(GT):
                    n = GT * f + t
                    if t == 1 and later:
                        y_parts(f - 2)
                    if later or half or t:
                        probs_part((t + 1) % 2, n - 1)
                    dve.wait_ge(scores_made, n + 1)
                    dve.tensor_reduce(row_max[:, t % 2:t % 2 + 1],
                                      ps[:, S_BANK + 2 * (t % 2):S_BANK + 2 * (t % 2) + 2, :].rearrange(
                                          "p a n -> p (a n)"),
                                      AX.X, ALU.max).then_inc(max_ready, 1)
                    if t == 0:
                        dve.tensor_copy(exp_scale[:, half:half + 1], score_scale[:, bass.ds(k // HEADS, 1)])
                    dve.wait_ge(max_ready, n + 1)
                    dve.tensor_scalar(exp_bias[:, t % 2:t % 2 + 1], row_max[:, t % 2:t % 2 + 1],
                                      neg_scale[:, bass.ds(k // HEADS, 1)], PROB_SHIFT, ALU.mult,
                                      ALU.add).then_inc(exp_bias_ready, 1)
                    if t == 1 and later:
                        row_factors(k if half else k - 1, f - 1, 1 - half)
                    if t < 2 and not (last and half):
                        q_part(1 - half, t, 2 * f + 3 + t)
                    if t >= 2 and later:
                        add_out(k - 1, f - 2, half, t - 2)
                    if prep and half and t == 2:
                        xt_quarter(XT_BANK, (((k // HEADS) + 1) % 2) * 2, k % HEADS, k + HEADS + 1)
                    if not later:
                        extras(n)

            def pair(k, later, prep, last):
                phase(k, 0, later, prep, last)
                phase(k, 1, later, prep, last)

            pair(0, False, True, False)
            finish_start()
            with dve.Fori(1, PAIRS - HEADS) as k:
                pair(k, True, True, False)
            with dve.Fori(PAIRS - HEADS, PAIRS - 1) as k:
                pair(k, True, False, False)
            pair(PAIRS - 1, True, False, True)
            f = 2 * PAIRS
            probs_part(1, GT * f - 1)
            y_parts(f - 2)
            row_factors(PAIRS - 1, f - 1, 1)

            def last_add(g, half, q, bank):
                dve.wait_ge(out_made, 2 * g + q // 2 + 1)
                dve.wait_ge(fac_ready, g + 1)
                dve.wait_ge(added, 1 + GT * g)
                o = ((B - 1) * JT + half * GT + q) * C
                dve.scalar_tensor_tensor(out=x_res[:, o:o + C], in0=ps[:, bank, 0:C],
                                         scalar=row_fac[:, half, q:q + 1], in1=x_res[:, o:o + C], op0=ALU.mult,
                                         op1=ALU.add).then_inc(added, 1)

            for q in range(GT):
                last_add(f - 2, 0, q, PREV_BANKS[q])
            y_parts(f - 1)
            for q in range(GT):
                last_add(f - 1, 1, q, LAST_BANKS[q])

        @block.gpsimd
        def _(pool):
            pool.memset(ones[:], 1.0).then_inc(const_ready, 1)
            pool.memset(ident[:], 0.0).then_inc(const_ready, 1)
            pool.wait_ge(const_ready, 2)
            pool.affine_select(out=ident[:], in_=ident[:], compare_op=ALU.not_equal, fill=1.0, base=0,
                               pattern=[[-1, P]], channel_multiplier=1).then_inc(const_ready, 1)
            pool.wait_ge(stage0_ready, 1)
            for q in range(HEADS):
                cut = slice(q * QT_TILES * C, (q + 1) * QT_TILES * C)
                low = slice(XSIZE + cut.start, XSIZE + cut.stop)
                pool.tensor_copy(x_nat[:, cut], stage0[:, cut]).then_inc(xn_high, 1)
                pool.wait_ge(xn_high, q + 1)
                pool.tensor_tensor(x_nat[:, low], stage0[:, cut], x_nat[:, cut], ALU.subtract).then_inc(xn_split, 1)
            pool.wait_ge(bias_in, 16)
            img0 = x_res[:, 0:JT * C].rearrange("p (t c) -> p t c", c=C)
            pool.tensor_tensor(img0, img0, bias[:, None, :].to_broadcast([P, JT, C]), ALU.add).then_inc(added, 1)

            def prepare(k, later, scales):
                size = QT_TILES * C
                src = x_res[:, bass.ds((k + HEADS) * size, size)]
                o = (((k // HEADS) + 1) % 2) * (2 * XSIZE) + (k % HEADS) * size
                pool.wait_ge(x_scale_ready, scales)
                pool.tensor_copy(raw[:], src).then_inc(raw_ready, 1)
                pool.tensor_copy(pool_scale[:], x_scale[:, bass.ds((k // HEADS) + 1, 1)]).then_inc(
                    pool_scale_ready, 1)
                pool.wait_ge(x_turned, k + HEADS)
                pool.wait_ge(raw_ready, k + 1)
                pool.wait_ge(pool_scale_ready, k + 1)
                pool.tensor_tensor(stage[:], raw[:], pool_scale[:].to_broadcast([P, size]),
                                   ALU.mult).then_inc(stage_ready, 1)
                pool.wait_ge(bias_in, 16)
                pool.tensor_tensor(src.rearrange("p (t c) -> p t c", c=C), raw[:].rearrange("p (t c) -> p t c", c=C),
                                   bias[:, None, :].to_broadcast([P, QT_TILES, C]), ALU.add).then_inc(bias_given, 1)
                pool.wait_ge(stage_ready, k + 1)
                if later:
                    pool.wait_ge(y_made, 4 * k)
                pool.tensor_copy(x_nat[:, bass.ds(o, size)], stage[:]).then_inc(xn_high, 1)
                pool.wait_ge(bias_given, k + 1)
                pool.wait_ge(xn_high, k + HEADS + 1)
                pool.tensor_tensor(x_nat[:, bass.ds(o + XSIZE, size)], stage[:], x_nat[:, bass.ds(o, size)],
                                   ALU.subtract).then_inc(xn_split, 1)
                pool.wait_ge(xn_split, k + HEADS + 1)

            prepare(0, False, 1)
            m_scaled = wo[:].rearrange("p s c -> p (s c)")
            pool.wait_ge(m_made, HEADS)
            pool.wait_ge(m_scale_ready, 1)
            pool.tensor_tensor(m_scaled, m_raw, col(M_SCALE).to_broadcast([P, ASIZE]),
                               ALU.mult).then_inc(m_scaled_ready, 1)
            pool.wait_ge(m_scaled_ready, 1)
            pool.wait_ge(m_high, 1)
            pool.tensor_tensor(m_w[:, ASIZE:2 * ASIZE], m_scaled, m_w[:, 0:ASIZE],
                               ALU.subtract).then_inc(m_split, 1)
            with pool.Fori(1, HEADS) as k:
                prepare(k, True, 1)
            with pool.Fori(HEADS, PAIRS - HEADS) as k:
                prepare(k, True, 2)


_INS = ['x', 'L0_conv_W_qkv', 'L0_conv_W_out', 'L0_conv_b_out']
_OUTS = [((8, 32, 32, 256), 'float32')]


def kernel(**inputs):
    import numpy as _np
    import concourse.bacc as _bacc
    from concourse import mybir as _mybir
    from concourse.bass_utils import run_bass_kernel_spmd as _run

    nc = _bacc.Bacc("TRN2", target_bir_lowering=False, num_devices=1)
    arrays, args = {}, []
    for name in _INS:
        a = _np.ascontiguousarray(inputs[name])
        arrays[f"in_{name}_dram"] = a
        args.append(nc.dram_tensor(f"in_{name}_dram", a.shape, _mybir.dt.from_np(a.dtype), kind="ExternalInput").ap())
    for i, (shape, dtype) in enumerate(_OUTS):
        dt = _mybir.dt.from_np(_np.dtype(dtype))
        args.append(nc.dram_tensor(f"out_{i}_dram", shape, dt, kind="ExternalOutput").ap())
    attention(nc, *args)
    r = _run(nc, [arrays], core_ids=[0])
    got = tuple(r.results[0][f"out_{i}_dram"] for i in range(len(_OUTS)))
    return got[0]
```
